# Optimizing a Trainium2 kernel written in Bass

```python
import numpy as np
import jax
import jax.numpy as jnp

def _softmax(x, axis=-1):
    return jax.nn.softmax(x, axis=axis)

def _gelu(x):
    return jax.nn.gelu(x, approximate=True)

def _silu(x):
    return jax.nn.silu(x)

def _sigmoid(x):
    return jax.nn.sigmoid(x)

def _layernorm(x, axis=-1, eps=1e-05):
    m = jnp.mean(x, axis=axis, keepdims=True)
    v = jnp.var(x, axis=axis, keepdims=True)
    return (x - m) / jnp.sqrt(v + eps)

def _scatter_add(tgt, idx, src, axis=0):
    return tgt.at[idx].add(src)

def _segment_sum(src, seg, n):
    return jax.ops.segment_sum(src, seg, n)
kernel_name = 'mk_gnn_preln_d1_gnn_r32_3ea862'

def setup_inputs(seed: int=0):
    np.random.seed(seed)
    _w = jnp.asarray

    def _rec_inputs():
        import jax
        import jax.numpy as jnp
        _gk = jax.random.key(seed)
        x = -0.0002928 + 1 * jax.random.normal(jax.random.fold_in(_gk, 1), (512, 256), jnp.float32)
        _s = jax.random.randint(jax.random.fold_in(_gk, 2), (8192,), 0, 512, jnp.int32)
        _d = jax.random.randint(jax.random.fold_in(_gk, 3), (8192,), 0, 512, jnp.int32)
        _loop = jnp.arange(512, dtype=jnp.int32)
        src = jnp.concatenate([_s, _d, _loop])
        dst = jnp.concatenate([_d, _s, _loop])
        _o = jnp.argsort(dst, stable=True)
        src = src[_o]
        dst = dst[_o]
        return (x, src, dst)
    x, src, dst = _rec_inputs()

    def _L0_gnn_setup():
        import jax, jax.numpy as jnp
        import numpy as np
        N_NODES = 512
        N_EDGES = 8192
        D_IN = 256
        D_OUT = 256
        key = jax.random.key(seed)
        k1, k2, k3, k4 = jax.random.split(key, 4)
        x = jax.random.normal(k1, (N_NODES, D_IN), dtype=jnp.float32)
        edge_index = jax.random.randint(k2, (2, N_EDGES), 0, N_NODES, dtype=jnp.int64)
        limit = float(np.sqrt(6.0 / (D_IN + D_OUT)))
        W = jax.random.uniform(k3, (D_OUT, D_IN), minval=-limit, maxval=limit, dtype=jnp.float32)
        B = jax.random.normal(k4, (D_OUT, D_IN), dtype=jnp.float32) * 0.02
        return {'x': x, 'edge_index': edge_index, 'W': W, 'B': B}
    _L0_gnn_all = _L0_gnn_setup()
    _L0_gnn_in = {k: v for k, v in _L0_gnn_all.items() if k in ('W', 'B')}
    del _L0_gnn_all
    return {'x': x, 'src': src, 'dst': dst, 'L0_gnn_W': _L0_gnn_in['W'], 'L0_gnn_B': _L0_gnn_in['B']}

def reference(x, src, dst, L0_gnn_W, L0_gnn_B):
    import jax
    import jax.numpy as jnp

    def _L0_gnn_ref(x, edge_index, W, B):
        import jax, jax.numpy as jnp
        import numpy as np
        N_NODES = 512
        N_EDGES = 8192
        D_IN = 256
        D_OUT = 256
        N = x.shape[0]
        src = edge_index[0]
        dst = edge_index[1]
        A = jnp.zeros((N, N), dtype=x.dtype).at[dst, src].set(1.0)
        deg = jnp.bincount(dst, length=N).astype(x.dtype)
        inv_deg = 1.0 / jnp.where(deg == 0, 1.0, deg)
        propagated = inv_deg[:, None] * (A @ x)
        return propagated @ W.T + x @ B.T
    edge_index = jnp.stack([src, dst])
    h = jnp.maximum(_layernorm(x, axis=-1), 0.0)
    x = x + _L0_gnn_ref(h, edge_index, L0_gnn_W, L0_gnn_B)
    return x

_drawn_inputs = setup_inputs


def setup_inputs(seed=0):
    import zlib

    import numpy as np

    out = dict(_drawn_inputs(seed))
    spreads = {}
    factors = {}
    for name, (base, spread) in spreads.items():
        noise = np.random.default_rng([zlib.crc32(name.encode()), seed]).standard_normal(out[name].shape)
        drawn = base * np.exp(spread * noise) if base else spread * noise
        out[name] = jnp.asarray(drawn.astype(out[name].dtype))
    for name, factor in factors.items():
        out[name] = (out[name] * factor).astype(out[name].dtype)
    return out
```

```python
import concourse.bass as bass
import concourse.mybir as mybir

P = 128
N = 512
D = 256
E = 16896
KB = N // P
T = E // P
FC = D // P
WIN = 24
LO = WIN * KB
COLS = P * KB
EPS = 1e-5
CHUNKS = [3, 6, 9] + [12] * 9 + [6]
STARTS = [sum(CHUNKS[:c]) for c in range(len(CHUNKS) + 1)]


def window_base(t):
    return min(max(round((P * t + P / 2) * N / E - WIN / 2), 0), N - WIN)


def chunk_of(t):
    return max(c for c in range(len(CHUNKS)) if STARTS[c] <= t)


LAST_TILE = [max(t for t in range(T) if window_base(t) < P * (k + 1)) for k in range(KB)]


def build(nc, edges, x, wb, out):
    fp32, bf16, i32, i16 = mybir.dt.float32, mybir.dt.bfloat16, mybir.dt.int32, mybir.dt.int16
    ALU, ACT, AX = mybir.AluOpType, mybir.ActivationFunctionType, mybir.AxisListType

    sb = lambda name, shape, dt: nc.alloc_sbuf_tensor(name, shape, dt)
    pb = lambda name: nc.alloc_psum_tensor(name, [P, COLS], fp32)
    sem = lambda name: nc.alloc_semaphore(name)

    zeros = sb("zeros", [P, COLS], bf16)
    ones = sb("ones", [P, P], fp32)
    ident = sb("ident", [P, P], fp32)
    iota = sb("iota", [P, P], i16)
    iota_all = sb("iota_all", [P, KB * COLS], i16)
    base_i = sb("base_i", [P, T], i32)
    base = sb("base", [P, T], fp32)
    half = sb("half", [P, KB], fp32)
    ed = sb("ed", [P, 2, T], i32)
    hi = sb("hi", [P, T], i32)
    lo = sb("lo", [P, T], i32)
    hi2 = sb("hi2", [P, T, 2], i16)
    rel2 = sb("rel2", [P, T, 2], i16)
    key = sb("key", [P, T], fp32)
    off = sb("off", [P, T], fp32)
    outside = sb("outside", [P, T], fp32)
    n_out = sb("n_out", [P, 1], fp32)
    bad = sb("bad", [1, 1], i32)
    hi_hot = sb("hi_hot", [P, T, P], bf16)
    lo_hot = sb("lo_hot", [P, T, LO], bf16)
    lo_full = sb("lo_full", [P, KB * COLS], bf16)
    xs = sb("xs", [P, KB, D], fp32)
    xz = sb("xz", [P, KB, D], fp32)
    wbs = sb("wbs", [P, FC, 2 * D], fp32)
    scratch = sb("scratch", [P, 2 * KB, D], bf16)
    xsum = sb("xsum", [P, KB], fp32)
    nmean = sb("nmean", [P, KB], fp32)
    vsum = sb("vsum", [P, KB], fp32)
    var = sb("var", [P, KB], fp32)
    rstd = sb("rstd", [P, KB], fp32)
    g = sb("g", [P, KB, D], fp32)
    gT = sb("gT", [P, FC, N], fp32)
    y = sb("y", [P, KB, D], fp32)
    zs = sb("zs", [P, KB, D], fp32)
    cnt = sb("cnt", [P, KB, COLS], fp32)
    adj = sb("adj", [P, KB, P, KB], fp32)
    pairs = sb("pairs", [P, KB, P, 2], fp32)
    dsum = sb("dsum", [P, KB, P], fp32)
    degc = sb("degc", [P, KB], fp32)
    inv = sb("inv", [P, KB], fp32)
    res = sb("res", [P, KB, D], fp32)

    bank = [pb(f"bank{k}") for k in range(KB)]
    py = [pb(f"py{j}") for j in range(2)]
    pz = [pb(f"pz{j}") for j in range(2)]

    s_x, s_e, s_w = sem("x_loaded"), sem("edges_loaded"), sem("weights_loaded")
    s_zero, s_iota, s_ident, s_basei, s_half = (sem(n) for n in (
        "zeros_ready", "iota_ready", "ident_ready", "base_iota", "half_ready"))
    s_prep, s_hi, s_lo = sem("dve_prep"), sem("hi_ready"), sem("lo_ready")
    s_sum, s_mean, s_g, s_sq, s_var, s_rstd = (sem(n) for n in (
        "xsum_ready", "mean_ready", "g_ready", "square_ready", "var_ready", "rstd_ready"))
    s_gt, s_gtc, s_y, s_yc, s_z, s_zc, s_xz = (sem(n) for n in (
        "gT_in_psum", "gT_ready", "y_in_psum", "y_ready", "z_in_psum", "z_ready", "xz_ready"))
    s_counts, s_cnt, s_adj, s_dsum, s_prod, s_deg, s_inv, s_res, s_out = (sem(n) for n in (
        "counts_in_psum", "counts_ready", "adj_ready", "degree_sums", "product_in_psum",
        "degrees_clamped", "inv_ready", "result_ready", "out_written"))
    s_pair = sem("degree_pairs")
    s_bp, s_bad, s_full, s_used, s_iall = (sem(n) for n in (
        "bad_in_psum", "bad_ready", "full_window_ready", "full_window_used", "iota_all_ready"))

    xv = x.rearrange("(k p) f -> p k f", p=P)
    ov = out.rearrange("(k p) f -> p k f", p=P)
    wv = wb.rearrange("(c p) f -> p c f", p=P)

    with nc.Block() as block:

        @block.sync
        def _(sp):
            sp.dma_start(ed[:, :, :], edges).then_inc(s_e, 16)
            sp.dma_start(wbs[:, :, :], wv).then_inc(s_w, 16)

            def store(k, rnd):
                sp.wait_ge(s_res, rnd * KB + k + 1)
                sp.dma_start(ov[:, k, :], res[:, k, :]).then_inc(s_out, 16)

            for k in range(KB):
                store(k, 0)
            sp.wait_ge(s_out, 16 * KB)
            sp.wait_ge(s_bad, 1)
            with sp.If(sp.value_load(bad[0:1, 0:1], min_val=0, max_val=E) > 0):
                for k in range(KB):
                    store(k, 1)
                sp.wait_ge(s_out, 32 * KB)

        @block.gpsimd
        def _(pool):
            pool.memset(zeros[:, :], 0.0).then_inc(s_zero, 1)
            pool.iota(base_i[:, :], [[P, T]], base=P // 2, channel_multiplier=0).then_inc(s_basei, 1)
            pool.iota(iota[:, :], [[1, P]], base=0, channel_multiplier=0,
                      allow_small_or_imprecise_dtypes=True).then_inc(s_iota, 1)
            pool.memset(ones[:, :], 1.0).then_inc(s_ident, 1)
            pool.memset(half[:, :], -0.5).then_inc(s_half, 1)
            pool.wait_ge(s_ident, 1)
            pool.affine_select(ident[:, :], ones[:, :], [[-1, P]], ALU.is_equal, 0.0, base=0,
                               channel_multiplier=1).then_inc(s_ident, 1)
            pool.wait_ge(s_sum, 1)
            pool.tensor_scalar(nmean[:, :], xsum[:, :], -1.0 / D, None, ALU.mult).then_inc(s_mean, 1)
            pool.wait_ge(s_sq, 1)
            pool.tensor_scalar(var[:, :], vsum[:, :], 1.0 / D, EPS, ALU.mult, ALU.add).then_inc(s_var, 1)
            pool.wait_ge(s_var, 1)
            pool.wait_ge(s_half, 1)
            pool.tensor_tensor(rstd[:, :], var[:, :], half[:, :], ALU.pow).then_inc(s_rstd, 1)

            def residual(k):
                pool.wait_ge(s_zc, k + 1)
                pool.tensor_tensor(xz[:, k, :], xs[:, k, :], zs[:, k, :], ALU.add).then_inc(s_xz, 1)

            def degree_sum(k, rnd):
                pool.wait_ge(s_cnt, rnd * KB + k + 1)
                if rnd:
                    pool.wait_ge(s_prod, KB)
                c = cnt[:, k, :].rearrange("p (d r) -> p d r", r=KB)
                pool.tensor_tensor(pairs[:, k, :, :], c[:, :, 0:2], c[:, :, 2:4], ALU.add).then_inc(s_pair, 1)
                pool.wait_ge(s_pair, rnd * KB + k + 1)
                pool.tensor_tensor(dsum[:, k, :], pairs[:, k, :, 0], pairs[:, k, :, 1],
                                   ALU.add).then_inc(s_dsum, 1)

            pool.wait_ge(s_x, 16)
            degree_sum(0, 0)
            for k in range(KB):
                residual(k)
            for k in range(1, KB):
                degree_sum(k, 0)
            pool.wait_ge(s_bad, 1)
            with pool.If(pool.value_load(bad[0:1, 0:1], min_val=0, max_val=E) > 0):
                pool.iota(iota_all[:, :], [[1, KB * COLS]], base=0, channel_multiplier=0,
                          allow_small_or_imprecise_dtypes=True).then_inc(s_iall, 1)
                for k in range(KB):
                    degree_sum(k, 1)

        @block.scalar
        def _(act):
            act.dma_start(xs[:, :, :], xv).then_inc(s_x, 16)
            act.wait_ge(s_x, 16)
            for k in range(KB):
                a = act.activation(scratch[:, k, :], xs[:, k, :], ACT.Copy, accum_out=xsum[:, k:k + 1])
            a.then_inc(s_sum, 1)
            act.wait_ge(s_mean, 1)
            for k in range(KB):
                act.activation(g[:, k, :], xs[:, k, :], ACT.Relu,
                               bias=nmean[:, k:k + 1]).then_inc(s_g, 1)
            for k in range(KB):
                a = act.activation(scratch[:, KB + k, :], xs[:, k, :], ACT.Square, bias=nmean[:, k:k + 1],
                                   accum_out=vsum[:, k:k + 1])
            a.then_inc(s_sq, 1)
            for j in range(FC):
                act.wait_ge(s_gt, j + 1)
                act.activation(gT[:, j, :], py[j][:, :], ACT.Copy).then_inc(s_gtc, 1)
            act.wait_ge(s_rstd, 1)

            def y_out(k):
                act.wait_ge(s_y, k // 2 + 1)
                act.activation(y[:, k, :], py[k // 2][:, k % 2 * D:k % 2 * D + D], ACT.Copy,
                               scale=rstd[:, k:k + 1]).then_inc(s_yc, 1)

            def z_out(k):
                act.wait_ge(s_z, k // 2 + 1)
                act.activation(zs[:, k, :], pz[k // 2][:, k % 2 * D:k % 2 * D + D], ACT.Copy,
                               scale=rstd[:, k:k + 1]).then_inc(s_zc, 1)

            def counts_out(k, rnd):
                if rnd:
                    act.wait_ge(s_used, T + 1)
                else:
                    act.wait_ge(s_counts, k + 1)
                act.activation(cnt[:, k, :], bank[k][:, :], ACT.Copy).then_inc(s_cnt, 1)

            for k in range(KB):
                y_out(k)
            counts_out(0, 0)
            z_out(0)
            z_out(1)
            z_out(2)
            z_out(3)
            for k in range(1, KB):
                counts_out(k, 0)
            act.wait_ge(s_bad, 1)
            with act.If(act.value_load(bad[0:1, 0:1], min_val=0, max_val=E) > 0):
                for k in range(KB):
                    counts_out(k, 1)

        @block.vector
        def _(dve):
            dve.wait_ge(s_basei, 1)
            dve.tensor_scalar(base_i[:, :], base_i[:, :], N / E, -WIN / 2.0,
                              ALU.mult, ALU.add).then_inc(s_prep, 1)
            dve.wait_ge(s_prep, 1)
            dve.tensor_scalar(base[:, :], base_i[:, :], 0.0, float(N - WIN),
                              ALU.max, ALU.min).then_inc(s_prep, 1)
            dve.wait_ge(s_prep, 2)
            dve.tensor_scalar(base[:, :], base[:, :], float(KB), None, ALU.mult).then_inc(s_prep, 1)

            dve.wait_ge(s_e, 16)
            dve.tensor_scalar(hi[:, :], ed[:, 0, :], P - 1, None, ALU.bitwise_and).then_inc(s_prep, 1)
            dve.tensor_scalar(lo[:, :], ed[:, 0, :], P.bit_length() - 1, None,
                              ALU.arith_shift_right).then_inc(s_prep, 1)
            dve.wait_ge(s_prep, 4)
            dve.tensor_copy(hi2[:, :, :], hi[:, :, None].to_broadcast([P, T, 2])).then_inc(s_prep, 1)
            dve.wait_ge(s_prep, 5)
            dve.scalar_tensor_tensor(key[:, :], ed[:, 1, :], float(KB), lo[:, :],
                                     ALU.mult, ALU.add).then_inc(s_prep, 1)
            dve.wait_ge(s_prep, 7)
            dve.tensor_tensor(rel2[:, :, :], key[:, :, None].to_broadcast([P, T, 2]),
                              base[:, :, None].to_broadcast([P, T, 2]), ALU.subtract).then_inc(s_prep, 1)
            dve.wait_ge(s_iota, 1)
            dve.wait_ge(s_prep, 8)

            def one_hot(c, dst, idx, width, done):
                a, n, h = STARTS[c], CHUNKS[c], width // 2
                o = dst[:, a:a + n, :].rearrange("p t (h two) -> p t h two", two=2)
                i0 = iota[:, 0:width].rearrange("p (h two) -> p h two", two=2)[:, None, :, :] \
                    .to_broadcast([P, n, h, 2])
                i1 = idx[:, a:a + n, None, :].to_broadcast([P, n, h, 2])
                dve.tensor_tensor(o, i0, i1, ALU.is_equal).then_inc(done, 1)

            def adjacency(k, rnd):
                dve.wait_ge(s_cnt, rnd * KB + k + 1)
                if rnd:
                    dve.wait_ge(s_prod, KB)
                dve.tensor_scalar(adj[:, k, :, :], cnt[:, k, :].rearrange("p (d r) -> p d r", r=KB),
                                  1.0, None, ALU.min).then_inc(s_adj, 1)

            def result(k, rnd):
                n = rnd * KB + k
                dve.wait_ge(s_prod, n + 1)
                dve.tensor_scalar(degc[:, k:k + 1], bank[k][:, D:D + 1], 1.0, None,
                                  ALU.max).then_inc(s_deg, 1)
                dve.wait_ge(s_deg, n + 1)
                dve.reciprocal(inv[:, k:k + 1], degc[:, k:k + 1]).then_inc(s_inv, 1)
                dve.wait_ge(s_inv, n + 1)
                dve.wait_ge(s_xz, k + 1)
                if rnd:
                    dve.wait_ge(s_out, 16 * KB)
                dve.scalar_tensor_tensor(res[:, k, :], bank[k][:, 0:D], inv[:, k:k + 1],
                                         xz[:, k, :], ALU.mult, ALU.add).then_inc(s_res, 1)

            def count_outside():
                dve.tensor_scalar(off[:, :], rel2[:, :, 0], 0.0, LO - 1.0,
                                  ALU.max, ALU.min).then_inc(s_prep, 1)
                dve.wait_ge(s_prep, 9)
                dve.tensor_tensor(outside[:, :], off[:, :], rel2[:, :, 0], ALU.not_equal).then_inc(s_prep, 1)
                dve.wait_ge(s_prep, 10)
                dve.tensor_reduce(n_out[:, :], outside[:, :], AX.X, ALU.add).then_inc(s_prep, 1)

            adj_at = {chunk_of(min(LAST_TILE[k] + 8, T - 1)): k for k in range(KB - 1)}
            for c in range(len(CHUNKS)):
                one_hot(c, hi_hot, hi2, P, s_hi)
                one_hot(c, lo_hot, rel2, LO, s_lo)
                if c == 4:
                    count_outside()
                if c == 6:
                    dve.wait_ge(s_bp, 1)
                    dve.tensor_copy(bad[0:1, 0:1], pz[0][0:1, 0:1]).then_inc(s_bad, 1)
                if c in adj_at:
                    adjacency(adj_at[c], 0)
            for k in range(KB - 1):
                result(k, 0)
            adjacency(KB - 1, 0)
            result(KB - 1, 0)

            with dve.If(dve.value_load(bad[0:1, 0:1], min_val=0, max_val=E) > 0):
                dve.wait_ge(s_iall, 1)
                with dve.Fori(0, T) as t:
                    dve.wait_ge(s_used, t + 1)
                    dve.tensor_scalar(lo_full[:, :], iota_all[:, :], key[:, bass.ds(t, 1)], None,
                                      ALU.is_equal).then_inc(s_full, 1)
                for k in range(KB):
                    adjacency(k, 1)
                for k in range(KB):
                    result(k, 1)

        @block.tensor
        def _(pe):
            def clear_counts():
                for k in range(KB):
                    pe.matmul(bank[k][:, :], zeros[:, 0:P], zeros[:, :], start=True, stop=False,
                              skip_group_check=True)

            def tile(t):
                b = window_base(t)
                cut = min(WIN, (b // P + 1) * P - b)
                last = None
                for d0, d1 in ((0, cut), (cut, WIN)):
                    if d0 < d1:
                        k, c0 = (b + d0) // P, (b + d0) % P * KB
                        last = pe.matmul(bank[k][:, c0:c0 + (d1 - d0) * KB], hi_hot[:, t, :],
                                         lo_hot[:, t, d0 * KB:d1 * KB], start=False,
                                         stop=False, skip_group_check=True)
                if t in LAST_TILE:
                    last.then_inc(s_counts, 1)

            def transposes(j):
                for k in range(KB):
                    if j == 0:
                        pe.wait_ge(s_g, k + 1)
                    m = pe.transpose(py[j][:, k * P:(k + 1) * P], g[:, k, j * P:(j + 1) * P], ident[:, :])
                m.then_inc(s_gt, 1)

            def dense(k, ps, half, done):
                for j in range(FC):
                    m = pe.matmul(ps[k // 2][:, k % 2 * D:k % 2 * D + D], gT[:, j, k * P:(k + 1) * P],
                                  wbs[:, j, half * D:half * D + D], start=(j == 0), stop=(j == FC - 1))
                if k % 2:
                    m.then_inc(done, 1)

            def sum_outside():
                pe.wait_ge(s_prep, 11)
                pe.matmul(pz[0][0:1, 0:1], n_out[:, :], ones[:, 0:1], start=True, stop=True).then_inc(s_bp, 1)

            def product(k, rnd):
                n = rnd * KB + k
                pe.wait_ge(s_adj, n + 1)
                for r in range(KB):
                    pe.matmul(bank[k][:, 0:D], adj[:, k, :, r], y[:, r, :], start=(r == 0),
                              stop=(r == KB - 1))
                pe.wait_ge(s_dsum, n + 1)
                pe.matmul(bank[k][:, D:D + 1], dsum[:, k, :], ones[:, 0:1], start=True,
                          stop=True).then_inc(s_prod, 1)

            pe.wait_ge(s_zero, 1)
            clear_counts()
            pe.wait_ge(s_ident, 2)
            product_at = {}
            for c in range(len(CHUNKS)):
                pe.wait_ge(s_hi, c + 1)
                pe.wait_ge(s_lo, c + 1)
                for t in range(STARTS[c], STARTS[c + 1]):
                    tile(t)
                if c == 2:
                    transposes(0)
                    transposes(1)
                if c == 5:
                    sum_outside()
                if c == 3:
                    pe.wait_ge(s_w, 16)
                    pe.wait_ge(s_gtc, 2)
                    for k in range(KB):
                        dense(k, py, 0, s_y)
                if c == 6:
                    pe.wait_ge(s_bad, 1)
                    for k in range(KB):
                        dense(k, pz, 1, s_z)
                if c == 8:
                    pe.wait_ge(s_yc, KB)
                    product(0, 0)
                if c == 10:
                    product(1, 0)
            product(2, 0)
            product(3, 0)

            pe.wait_ge(s_bad, 1)
            with pe.If(pe.value_load(bad[0:1, 0:1], min_val=0, max_val=E) > 0):
                pe.wait_ge(s_res, KB)
                clear_counts()
                pe.nop().then_inc(s_used, 1)
                with pe.Fori(0, T) as t:
                    pe.wait_ge(s_full, t + 1)
                    for k in range(KB):
                        m = pe.matmul(bank[k][:, :], hi_hot[:, bass.ds(t, 1), :].rearrange("p a b -> p (a b)"),
                                      lo_full[:, k * COLS:(k + 1) * COLS], start=False,
                                      stop=False, skip_group_check=True)
                    m.then_inc(s_used, 1)
                for k in range(KB):
                    product(k, 1)


def kernel(**inputs):
    import numpy as np
    import concourse.bacc as bacc
    from concourse.bass_utils import run_bass_kernel_spmd

    x = np.ascontiguousarray(inputs["x"])
    w, b = np.asarray(inputs["L0_gnn_W"]), np.asarray(inputs["L0_gnn_B"])
    arrays = {
        "edges": np.ascontiguousarray(np.stack(
            [np.asarray(inputs[n]).reshape(T, P).T for n in ("src", "dst")], axis=1)),
        "x": x,
        "wb": np.ascontiguousarray(np.concatenate([w.T, b.T], axis=1)),
    }
    nc = bacc.Bacc("TRN2", target_bir_lowering=False, num_devices=1)
    aps = [nc.dram_tensor(n, a.shape, mybir.dt.from_np(a.dtype), kind="ExternalInput").ap()
           for n, a in arrays.items()]
    out = nc.dram_tensor("out", (N, D), mybir.dt.float32, kind="ExternalOutput").ap()
    build(nc, *aps, out)
    return run_bass_kernel_spmd(nc, [arrays], core_ids=[0]).results[0]["out"]
```

```python
import math

import concourse.bass as bass
import concourse.mybir as mybir

P = 128
N = 512
D = 256
E = 16896
KB = N // P
T = E // P
FC = D // P
COLS = P * KB
EPS = 1e-5
CHUNKS = [3, 6, 9] + [12] * 8 + [9, 6, 3]
STARTS = [sum(CHUNKS[:c]) for c in range(len(CHUNKS) + 1)]
SPREAD = 3.5


def centre(t):
    return (P * t + P / 2) * N / E


def width(c):
    at = [(t + 0.5) / T for t in range(STARTS[c], STARTS[c + 1])]
    stray = max((E - N) ** 0.5 * N / E * (s * (1 - s)) ** 0.5 for s in at)
    return 2 * math.ceil(P * N / E / 2 + 1 + SPREAD * (stray + 0.3))


WIDTHS = [width(c) for c in range(len(CHUNKS))]
LO_AT = [sum(n * w * KB for n, w in zip(CHUNKS[:c], WIDTHS)) for c in range(len(CHUNKS) + 1)]


def chunk_of(t):
    return max(c for c in range(len(CHUNKS)) if STARTS[c] <= t)


def window(t):
    w = WIDTHS[chunk_of(t)]
    return min(max(round(centre(t) - w / 2), 0), N - w), w


LAST_TILE = [max(t for t in range(T) if window(t)[0] < P * (k + 1)) for k in range(KB)]


def build(nc, edges, x, wb, out):
    fp32, bf16, i32, i16 = mybir.dt.float32, mybir.dt.bfloat16, mybir.dt.int32, mybir.dt.int16
    ALU, ACT, AX = mybir.AluOpType, mybir.ActivationFunctionType, mybir.AxisListType

    sb = lambda name, shape, dt: nc.alloc_sbuf_tensor(name, shape, dt)
    pb = lambda name: nc.alloc_psum_tensor(name, [P, COLS], fp32)
    sem = lambda name: nc.alloc_semaphore(name)

    zeros = sb("zeros", [P, COLS], bf16)
    ones = sb("ones", [P, P], fp32)
    ident = sb("ident", [P, P], fp32)
    iota = sb("iota", [P, P], i16)
    iota_all = sb("iota_all", [P, KB * COLS], i16)
    base_i = sb("base_i", [P, T], i32)
    base = sb("base", [P, T], fp32)
    half = sb("half", [P, KB], fp32)
    ed = sb("ed", [P, 2, T], i32)
    lo = sb("lo", [P, T], i16)
    hi2 = sb("hi2", [P, T, 2], i16)
    rel2 = sb("rel2", [P, T, 2], i16)
    key = sb("key", [P, T], fp32)
    off = sb("off", [P, 2, T], fp32)
    unread = sb("unread", [P, 2, T], bf16)
    n_out = sb("n_out", [P, 1], fp32)
    bad = sb("bad", [1, 1], i32)
    hi_hot = sb("hi_hot", [P, T, P], bf16)
    lo_hot = sb("lo_hot", [P, LO_AT[-1]], bf16)
    lo_full = sb("lo_full", [P, KB * COLS], bf16)
    xs = sb("xs", [P, KB, D], fp32)
    xz = sb("xz", [P, KB, D], fp32)
    wbs = sb("wbs", [P, FC, 2 * D], fp32)
    scratch = sb("scratch", [P, 2 * KB, D], bf16)
    nmean = sb("nmean", [P, KB], fp32)
    vsum = sb("vsum", [P, KB], fp32)
    var = sb("var", [P, KB], fp32)
    rstd = sb("rstd", [P, KB], fp32)
    g = sb("g", [P, KB, D], fp32)
    gT = sb("gT", [P, FC, N], fp32)
    parts = [sb(f"y{i}", [P, KB, D], fp32) for i in range(3)]
    upper = [t[:, :, :].bitcast(bf16).rearrange("p k (d h) -> p k d h", h=2)[:, :, :, 1] for t in parts]
    cnt = sb("cnt", [P, KB, COLS], fp32)
    adj = sb("adj", [P, KB, P, KB], bf16)
    pairs = sb("pairs", [P, KB, P, 2], fp32)
    dsum = sb("dsum", [P, KB, P], fp32)
    degc = sb("degc", [P, KB], fp32)
    inv = sb("inv", [P, KB], fp32)
    res = sb("res", [P, KB, D], fp32)

    bank = [pb(f"bank{k}") for k in range(KB)]
    py = [pb(f"py{j}") for j in range(2)]
    pz = [pb(f"pz{j}") for j in range(2)]

    s_x, s_e, s_w = [sem("x01_loaded"), sem("x23_loaded")], sem("edges_loaded"), sem("weights_loaded")
    s_zero, s_iota, s_ident, s_basei, s_half = (sem(n) for n in (
        "zeros_ready", "iota_ready", "ident_ready", "base_iota", "half_ready"))
    s_prep, s_rel, s_hi, s_lo = (sem(n) for n in ("dve_prep", "rel_ready", "hi_ready", "lo_ready"))
    s_off, s_nout = sem("outside_steps"), sem("n_out_ready")
    s_mean, s_g, s_sq, s_var, s_rstd = (sem(n) for n in (
        "mean_ready", "g_ready", "square_ready", "var_ready", "rstd_ready"))
    s_gt, s_gtc, s_y, s_yc, s_y1, s_y2, s_z, s_xz = (sem(n) for n in (
        "gT_in_psum", "gT_ready", "y_in_psum", "y_ready", "y_first_rest",
        "y_second_rest", "z_in_psum", "xz_ready"))
    s_counts, s_cnt, s_adj, s_dsum, s_prod, s_deg, s_inv, s_res, s_out = (sem(n) for n in (
        "counts_in_psum", "counts_ready", "adj_ready", "degree_sums", "product_in_psum",
        "degrees_clamped", "inv_ready", "result_ready", "out_written"))
    s_pair = sem("degree_pairs")
    s_bp, s_bad, s_full, s_used, s_iall = (sem(n) for n in (
        "bad_in_psum", "bad_ready", "full_window_ready", "full_window_used", "iota_all_ready"))

    xv = x.rearrange("(k p) f -> p k f", p=P)
    ov = out.rearrange("(k p) f -> p k f", p=P)
    wv = wb.rearrange("(c p) f -> p c f", p=P)

    with nc.Block() as block:

        @block.sync
        def _(sp):
            sp.dma_start(ed[:, :, :], edges).then_inc(s_e, 16)
            sp.dma_start(xs[:, 2:KB, :], xv[:, 2:KB, :]).then_inc(s_x[1], 16)
            sp.dma_start(wbs[:, :, :], wv).then_inc(s_w, 16)

            def store(k, rnd):
                sp.wait_ge(s_res, rnd * KB + k + 1)
                sp.dma_start(ov[:, k, :], res[:, k, :]).then_inc(s_out, 16)

            for k in range(KB):
                store(k, 0)
            sp.wait_ge(s_out, 16 * KB)
            sp.wait_ge(s_bad, 1)
            with sp.If(sp.value_load(bad[0:1, 0:1], min_val=0, max_val=E) > 0):
                for k in range(KB):
                    store(k, 1)
                sp.wait_ge(s_out, 32 * KB)

        @block.gpsimd
        def _(pool):
            pool.memset(zeros[:, :], 0.0).then_inc(s_zero, 1)
            pool.iota(base_i[:, :], [[P, T]], base=P // 2, channel_multiplier=0).then_inc(s_basei, 1)
            pool.iota(iota[:, :], [[1, P]], base=0, channel_multiplier=0,
                      allow_small_or_imprecise_dtypes=True).then_inc(s_iota, 1)
            pool.memset(ones[:, :], 1.0).then_inc(s_ident, 1)
            pool.memset(half[:, :], -0.5).then_inc(s_half, 1)
            pool.wait_ge(s_ident, 1)
            pool.affine_select(ident[:, :], ones[:, :], [[-1, P]], ALU.is_equal, 0.0, base=0,
                               channel_multiplier=1).then_inc(s_ident, 1)
            pool.wait_ge(s_rel, 1)
            for c in range(len(CHUNKS)):
                a, z, w = STARTS[c], STARTS[c + 1], WIDTHS[c] * KB - 1.0
                pool.tensor_scalar(off[:, 0, a:z], rel2[:, a:z, 0], w, w, ALU.max, ALU.subtract)
            pool.tensor_scalar(off[:, 1, :], rel2[:, :, 0], 0.0, -1.0, ALU.min,
                               ALU.mult).then_inc(s_off, 1)
            pool.wait_ge(s_sq, 1)
            pool.tensor_scalar(var[:, :], vsum[:, :], 1.0 / D, EPS, ALU.mult, ALU.add).then_inc(s_var, 1)
            pool.wait_ge(s_var, 1)
            pool.wait_ge(s_half, 1)
            pool.tensor_tensor(rstd[:, :], var[:, :], half[:, :], ALU.pow).then_inc(s_rstd, 1)

            def split(i, pair):
                ks = slice(2 * pair, 2 * pair + 2)
                pool.tensor_tensor(parts[i + 1][:, ks, :], parts[i][:, ks, :], upper[i][:, ks, :],
                                   ALU.subtract).then_inc((s_y1, s_y2)[i], 1)

            def degree_sum(k, rnd):
                pool.wait_ge(s_cnt, rnd * KB + k + 1)
                if rnd:
                    pool.wait_ge(s_prod, KB)
                c = cnt[:, k, :].rearrange("p (d r) -> p d r", r=KB)
                pool.tensor_tensor(pairs[:, k, :, :], c[:, :, 0:2], c[:, :, 2:4], ALU.add).then_inc(s_pair, 1)
                pool.wait_ge(s_pair, rnd * KB + k + 1)
                pool.tensor_tensor(dsum[:, k, :], pairs[:, k, :, 0], pairs[:, k, :, 1],
                                   ALU.add).then_inc(s_dsum, 1)

            degree_sum(0, 0)
            for pair in range(2):
                pool.wait_ge(s_yc, 2 * pair + 2)
                split(0, pair)
                pool.wait_ge(s_y1, pair + 1)
                split(1, pair)
            for k in range(1, KB):
                degree_sum(k, 0)
            pool.wait_ge(s_bad, 1)
            with pool.If(pool.value_load(bad[0:1, 0:1], min_val=0, max_val=E) > 0):
                pool.iota(iota_all[:, :], [[1, KB * COLS]], base=0, channel_multiplier=0,
                          allow_small_or_imprecise_dtypes=True).then_inc(s_iall, 1)
                for k in range(KB):
                    degree_sum(k, 1)

        @block.scalar
        def _(act):
            act.dma_start(xs[:, 0:2, :], xv[:, 0:2, :]).then_inc(s_x[0], 16)
            for k in range(KB):
                act.wait_ge(s_x[k // 2], 16)
                act.activation(scratch[:, k, :], xs[:, k, :], ACT.Copy, scale=-1.0 / D,
                               accum_out=nmean[:, k:k + 1]).then_inc(s_mean, 1)
            for k in range(KB):
                act.wait_ge(s_mean, k + 1)
                a = act.activation(scratch[:, KB + k, :], xs[:, k, :], ACT.Square, bias=nmean[:, k:k + 1],
                                   accum_out=vsum[:, k:k + 1])
            a.then_inc(s_sq, 1)
            for j in range(FC):
                act.wait_ge(s_gt, j + 1)
                act.activation(gT[:, j, :], py[j][:, :], ACT.Copy).then_inc(s_gtc, 1)

            def y_out(k):
                act.wait_ge(s_y, k // 2 + 1)
                act.activation(parts[0][:, k, :], py[k // 2][:, k % 2 * D:k % 2 * D + D], ACT.Copy,
                               scale=rstd[:, k:k + 1]).then_inc(s_yc, 1)

            def counts_out(k, rnd):
                if rnd:
                    act.wait_ge(s_used, T + 1)
                else:
                    act.wait_ge(s_counts, k + 1)
                act.activation(cnt[:, k, :], bank[k][:, :], ACT.Copy).then_inc(s_cnt, 1)
                if k < KB - 1 and not rnd:
                    act.activation(adj[:, k, :, :].rearrange("p d r -> p (d r)"), bank[k][:, :],
                                   ACT.Sign).then_inc(s_adj, 1)

            act.wait_ge(s_off, 1)
            act.activation(unread[:, :, :], off[:, :, :], ACT.Copy, accum_out=n_out[:, :]).then_inc(s_nout, 1)
            counts_out(0, 0)
            act.wait_ge(s_rstd, 1)
            y_out(0)
            y_out(1)
            act.wait_ge(s_bp, 1)
            act.activation(bad[0:1, 0:1], pz[0][0:1, 0:1], ACT.Copy).then_inc(s_bad, 1)
            y_out(2)
            y_out(3)
            for k in range(1, KB):
                counts_out(k, 0)
            act.wait_ge(s_bad, 1)
            with act.If(act.value_load(bad[0:1, 0:1], min_val=0, max_val=E) > 0):
                for k in range(KB):
                    counts_out(k, 1)

        @block.vector
        def _(dve):
            dve.wait_ge(s_basei, 1)
            for c in range(len(CHUNKS)):
                a, z = STARTS[c], STARTS[c + 1]
                last = dve.tensor_scalar(base_i[:, a:z], base_i[:, a:z], N / E, -WIDTHS[c] / 2.0,
                                         ALU.mult, ALU.add)
            last.then_inc(s_prep, 1)
            dve.wait_ge(s_prep, 1)
            dve.tensor_scalar(base[:, :], base_i[:, :], 0.0, float(N - WIDTHS[-1]),
                              ALU.max, ALU.min).then_inc(s_prep, 1)
            dve.wait_ge(s_prep, 2)
            dve.tensor_scalar(base[:, :], base[:, :], float(KB), None, ALU.mult).then_inc(s_prep, 1)

            dve.wait_ge(s_e, 16)
            low = ed[:, :, :].bitcast(i16).rearrange("p a (t h) -> p a t h", h=2)[:, 0, :, 0]
            dve.tensor_scalar(lo[:, :], low, P.bit_length() - 1, None,
                              ALU.logical_shift_right).then_inc(s_prep, 1)
            dve.tensor_scalar(hi2[:, :, :], low[:, :, None].to_broadcast([P, T, 2]), P - 1, None,
                              ALU.bitwise_and).then_inc(s_prep, 1)
            dve.wait_ge(s_prep, 4)
            dve.scalar_tensor_tensor(key[:, :], ed[:, 1, :], float(KB), lo[:, :],
                                     ALU.mult, ALU.add).then_inc(s_prep, 1)
            dve.wait_ge(s_iota, 1)

            def one_hot(c, out, idx, width):
                a, n, h = STARTS[c], CHUNKS[c], width // 2
                o = out.rearrange("p (t h two) -> p t h two", h=h, two=2)
                i0 = iota[:, 0:width].rearrange("p (h two) -> p h two", two=2)[:, None, :, :] \
                    .to_broadcast([P, n, h, 2])
                i1 = idx[:, a:a + n, None, :].to_broadcast([P, n, h, 2])
                return dve.tensor_tensor(o, i0, i1, ALU.is_equal)

            def hi_one_hot(c):
                one_hot(c, hi_hot[:, STARTS[c]:STARTS[c + 1], :].rearrange("p t h -> p (t h)"),
                        hi2, P).then_inc(s_hi, 1)

            def lo_one_hot(c):
                one_hot(c, lo_hot[:, LO_AT[c]:LO_AT[c + 1]], rel2, WIDTHS[c] * KB).then_inc(s_lo, 1)

            def residual(k):
                dve.wait_ge(s_rstd, 1)
                dve.wait_ge(s_z, k // 2 + 1)
                dve.scalar_tensor_tensor(xz[:, k, :], pz[k // 2][:, k % 2 * D:k % 2 * D + D],
                                         rstd[:, k:k + 1], xs[:, k, :], ALU.mult,
                                         ALU.add).then_inc(s_xz, 1)

            def adjacency(k, rnd):
                dve.wait_ge(s_cnt, rnd * KB + k + 1)
                if rnd:
                    dve.wait_ge(s_prod, KB)
                dve.tensor_scalar(adj[:, k, :, :], cnt[:, k, :].rearrange("p (d r) -> p d r", r=KB),
                                  1.0, None, ALU.min).then_inc(s_adj, 1)

            def result(k, rnd):
                n = rnd * KB + k
                dve.wait_ge(s_prod, n + 1)
                dve.tensor_scalar(degc[:, k:k + 1], bank[k][:, D:D + 1], 1.0, None,
                                  ALU.max).then_inc(s_deg, 1)
                dve.wait_ge(s_deg, n + 1)
                dve.reciprocal(inv[:, k:k + 1], degc[:, k:k + 1]).then_inc(s_inv, 1)
                dve.wait_ge(s_inv, n + 1)
                dve.wait_ge(s_xz, k + 1)
                if rnd:
                    dve.wait_ge(s_out, 16 * KB)
                dve.scalar_tensor_tensor(res[:, k, :], bank[k][:, 0:D], inv[:, k:k + 1],
                                         xz[:, k, :], ALU.mult, ALU.add).then_inc(s_res, 1)

            dve.wait_ge(s_prep, 5)
            hi_one_hot(0)
            dve.wait_ge(s_prep, 6)
            dve.tensor_tensor(rel2[:, :, :], key[:, :, None].to_broadcast([P, T, 2]),
                              base[:, :, None].to_broadcast([P, T, 2]), ALU.subtract).then_inc(s_rel, 1)
            hi_one_hot(1)
            dve.wait_ge(s_rel, 1)
            lo_one_hot(0)
            lo_one_hot(1)
            hi_one_hot(2)
            lo_one_hot(2)
            for k in range(KB):
                dve.wait_ge(s_mean, k + 1)
                dve.tensor_scalar(g[:, k, :], xs[:, k, :], nmean[:, k:k + 1], 0.0, ALU.add,
                                  ALU.max).then_inc(s_g, 1)
            for c in range(3, len(CHUNKS)):
                hi_one_hot(c)
                lo_one_hot(c)
                if c == 9:
                    residual(0)
                    residual(1)
            residual(2)
            residual(3)
            adjacency(KB - 1, 0)
            for k in range(KB):
                result(k, 0)

            with dve.If(dve.value_load(bad[0:1, 0:1], min_val=0, max_val=E) > 0):
                dve.wait_ge(s_iall, 1)
                with dve.Fori(0, T) as t:
                    dve.wait_ge(s_used, t + 1)
                    dve.tensor_scalar(lo_full[:, :], iota_all[:, :], key[:, bass.ds(t, 1)], None,
                                      ALU.is_equal).then_inc(s_full, 1)
                for k in range(KB):
                    adjacency(k, 1)
                for k in range(KB):
                    result(k, 1)

        @block.tensor
        def _(pe):
            def clear_counts():
                for k in range(KB):
                    pe.matmul(bank[k][:, :], zeros[:, 0:P], zeros[:, :], start=True, stop=False,
                              skip_group_check=True)

            def tile(t):
                c, (b, w) = chunk_of(t), window(t)
                at = LO_AT[c] + (t - STARTS[c]) * w * KB
                cut = min(w, (b // P + 1) * P - b)
                for d0, d1 in ((0, cut), (cut, w)):
                    if d0 < d1:
                        k, c0 = (b + d0) // P, (b + d0) % P * KB
                        last = pe.matmul(bank[k][:, c0:c0 + (d1 - d0) * KB], hi_hot[:, t, :],
                                         lo_hot[:, at + d0 * KB:at + d1 * KB], start=False,
                                         stop=False, skip_group_check=True)
                if t in LAST_TILE:
                    last.then_inc(s_counts, 1)

            def transposes(j):
                for k in range(KB):
                    if j == 0:
                        pe.wait_ge(s_g, k + 1)
                    m = pe.transpose(py[j][:, k * P:(k + 1) * P], g[:, k, j * P:(j + 1) * P], ident[:, :])
                m.then_inc(s_gt, 1)

            def dense(k, ps, half, done):
                for j in range(FC):
                    m = pe.matmul(ps[k // 2][:, k % 2 * D:k % 2 * D + D], gT[:, j, k * P:(k + 1) * P],
                                  wbs[:, j, half * D:half * D + D], start=(j == 0), stop=(j == FC - 1))
                if k % 2:
                    m.then_inc(done, 1)

            def sum_outside():
                pe.wait_ge(s_nout, 1)
                pe.matmul(pz[0][0:1, 0:1], n_out[:, :], ones[:, 0:1], start=True, stop=True).then_inc(s_bp, 1)

            def product(k, rnd):
                n = rnd * KB + k
                pe.wait_ge(s_adj, n + 1)
                for i in range(3):
                    for r in range(KB):
                        if r % 2 == 0:
                            pe.wait_ge((s_yc, s_y1, s_y2)[i], (r + 2, r // 2 + 1)[i > 0])
                        pe.matmul(bank[k][:, 0:D], adj[:, k, :, r], upper[i][:, r, :],
                                  start=(i == 0 and r == 0), stop=(i == 2 and r == KB - 1))
                pe.wait_ge(s_dsum, n + 1)
                pe.matmul(bank[k][:, D:D + 1], dsum[:, k, :], ones[:, 0:1], start=True,
                          stop=True).then_inc(s_prod, 1)

            def tiles(*chunks):
                for c in chunks:
                    pe.wait_ge(s_hi, c + 1)
                    pe.wait_ge(s_lo, c + 1)
                    for t in range(STARTS[c], STARTS[c + 1]):
                        tile(t)

            pe.wait_ge(s_zero, 1)
            clear_counts()
            pe.wait_ge(s_ident, 2)
            tiles(0, 1, 2)
            transposes(0)
            transposes(1)
            tiles(3)
            pe.wait_ge(s_w, 16)
            pe.wait_ge(s_gtc, 2)
            dense(0, py, 0, s_y)
            dense(1, py, 0, s_y)
            tiles(4)
            sum_outside()
            dense(2, py, 0, s_y)
            dense(3, py, 0, s_y)
            tiles(5, 6)
            pe.wait_ge(s_bad, 1)
            dense(0, pz, 1, s_z)
            dense(1, pz, 1, s_z)
            tiles(7, 8)
            product(0, 0)
            dense(2, pz, 1, s_z)
            dense(3, pz, 1, s_z)
            tiles(9, 10)
            product(1, 0)
            tiles(11, 12, 13)
            product(2, 0)
            product(3, 0)

            pe.wait_ge(s_bad, 1)
            with pe.If(pe.value_load(bad[0:1, 0:1], min_val=0, max_val=E) > 0):
                pe.wait_ge(s_res, KB)
                clear_counts()
                pe.nop().then_inc(s_used, 1)
                with pe.Fori(0, T) as t:
                    pe.wait_ge(s_full, t + 1)
                    for k in range(KB):
                        m = pe.matmul(bank[k][:, :], hi_hot[:, bass.ds(t, 1), :].rearrange("p a b -> p (a b)"),
                                      lo_full[:, k * COLS:(k + 1) * COLS], start=False,
                                      stop=False, skip_group_check=True)
                    m.then_inc(s_used, 1)
                for k in range(KB):
                    product(k, 1)


def kernel(**inputs):
    import numpy as np
    import concourse.bacc as bacc
    from concourse.bass_utils import run_bass_kernel_spmd

    x = np.ascontiguousarray(inputs["x"])
    w, b = np.asarray(inputs["L0_gnn_W"]), np.asarray(inputs["L0_gnn_B"])
    arrays = {
        "edges": np.ascontiguousarray(np.stack(
            [np.asarray(inputs[n]).reshape(T, P).T for n in ("src", "dst")], axis=1)),
        "x": x,
        "wb": np.ascontiguousarray(np.concatenate([w.T, b.T], axis=1)),
    }
    nc = bacc.Bacc("TRN2", target_bir_lowering=False, num_devices=1)
    aps = [nc.dram_tensor(n, a.shape, mybir.dt.from_np(a.dtype), kind="ExternalInput").ap()
           for n, a in arrays.items()]
    out = nc.dram_tensor("out", (N, D), mybir.dt.float32, kind="ExternalOutput").ap()
    build(nc, *aps, out)
    return run_bass_kernel_spmd(nc, [arrays], core_ids=[0]).results[0]["out"]
```

```python
import math

import concourse.bass as bass
import concourse.mybir as mybir

P = 128
N = 512
D = 256
E = 16896
KB = N // P
T = E // P
FC = D // P
COLS = P * KB
EPS = 1e-5
CHUNKS = [3, 6, 9] + [12] * 9 + [6]
STARTS = [sum(CHUNKS[:c]) for c in range(len(CHUNKS) + 1)]
CLEARS = 2
ROUND = 1.5 * 2 ** 23
SPREAD = 3.5


def centre(t):
    return (P * t + P / 2) * N / E


def width(c):
    at = [(t + 0.5) / T for t in range(STARTS[c], STARTS[c + 1])]
    stray = max((E - N) ** 0.5 * N / E * (s * (1 - s)) ** 0.5 for s in at)
    return 2 * math.ceil(P * N / E / 2 + 0.5 + SPREAD * (stray + 0.15))


WIDTHS = [width(c) for c in range(len(CHUNKS))]
RUNS = [(STARTS[c], STARTS[e], w) for c, e, w in (
    (c, next((e for e in range(c, len(WIDTHS)) if WIDTHS[e] != w), len(WIDTHS)), w)
    for c, w in enumerate(WIDTHS) if c == 0 or WIDTHS[c - 1] != w)]
LO_AT = [sum(n * w * KB for n, w in zip(CHUNKS[:c], WIDTHS)) for c in range(len(CHUNKS) + 1)]


def chunk_of(t):
    return max(c for c in range(len(CHUNKS)) if STARTS[c] <= t)


def window(t):
    w = WIDTHS[chunk_of(t)]
    return min(max(round(centre(t) - w / 2), 0), N - w), w


assert all(window(t)[0] + window(t)[1] < N for t in range(STARTS[-2]))
LAST_TILE = [max(t for t in range(T) if window(t)[0] < P * (k + 1)) for k in range(KB)]


def build(nc, edges, x, wb, out):
    fp32, bf16, i32, i16 = mybir.dt.float32, mybir.dt.bfloat16, mybir.dt.int32, mybir.dt.int16
    ALU, ACT, AX = mybir.AluOpType, mybir.ActivationFunctionType, mybir.AxisListType

    sb = lambda name, shape, dt: nc.alloc_sbuf_tensor(name, shape, dt)
    pb = lambda name: nc.alloc_psum_tensor(name, [P, COLS], fp32)
    sem = lambda name: nc.alloc_semaphore(name)

    zeros = sb("zeros", [P, COLS], bf16)
    one = sb("one", [P, 1], bf16)
    ones = sb("ones", [P, P], fp32)
    ident = sb("ident", [P, P], fp32)
    iota = sb("iota", [P, P], i16)
    iota_all = sb("iota_all", [P, KB * COLS], i16)
    middle = sb("middle", [P, T], i32)
    base = sb("base", [P, T], fp32)
    half = sb("half", [P, KB], fp32)
    ed = sb("ed", [P, 2, T], i32)
    lo = sb("lo", [P, T], i16)
    hi2 = sb("hi2", [P, T, 2], i16)
    rel2 = sb("rel2", [P, T, 2], i16)
    key = sb("key", [P, T], fp32)
    counted = sb("counted", [1, 1], i32)
    hi_hot = sb("hi_hot", [P, T, P], bf16)
    lo_hot = sb("lo_hot", [P, LO_AT[-1]], bf16)
    lo_full = sb("lo_full", [P, KB * COLS], bf16)
    xs = sb("xs", [P, KB, D], fp32)
    zs = sb("zs", [P, KB, D], fp32)
    xz = sb("xz", [P, KB, D], fp32)
    wbs = sb("wbs", [P, FC, 2 * D], fp32)
    scratch = sb("scratch", [P, 2 * KB, D], bf16)
    nmean = sb("nmean", [P, KB], fp32)
    vsum = sb("vsum", [P, KB], fp32)
    var = sb("var", [P, KB], fp32)
    rstd = sb("rstd", [P, KB], fp32)
    g = sb("g", [P, KB, D], fp32)
    gT = sb("gT", [P, KB // 2, FC, 2 * P], fp32)
    parts = [sb(f"y{i}", [P, KB, D], fp32) for i in range(3)]
    upper = [t[:, :, :].bitcast(bf16).rearrange("p k (d h) -> p k d h", h=2)[:, :, :, 1] for t in parts]
    cnt = sb("cnt", [P, KB, COLS], fp32)
    csum = sb("csum", [P, KB], fp32)
    totals = sb("totals", [1, KB], fp32)
    total = sb("total", [1, 1], fp32)
    adj = sb("adj", [P, KB, P, KB], bf16)
    pairs = sb("pairs", [P, KB, P, 2], fp32)
    dsum = sb("dsum", [P, KB, P], fp32)
    drest = sb("drest", [P, KB, P], bf16)
    dtop = dsum[:, :, :].bitcast(bf16).rearrange("p k (d h) -> p k d h", h=2)[:, :, :, 1]
    degc = sb("degc", [P, KB], fp32)
    inv = sb("inv", [P, KB], fp32)
    res = sb("res", [P, KB, D], fp32)

    bank = [pb(f"bank{k}") for k in range(KB)]
    py = [pb(f"py{j}") for j in range(2)]
    pz = [pb(f"pz{j}") for j in range(2)]

    s_x, s_e, s_w = [sem("x01_loaded"), sem("x23_loaded")], sem("edges_loaded"), sem("weights_loaded")
    s_zero, s_iota, s_ident, s_middle, s_half = (sem(n) for n in (
        "zeros_ready", "iota_ready", "ident_ready", "middle_ready", "half_ready"))
    s_prep, s_rel, s_hi, s_lo = (sem(n) for n in ("dve_prep", "rel_ready", "hi_ready", "lo_ready"))
    s_total = sem("total_ready")
    s_mean, s_g, s_sq, s_var, s_rstd = (sem(n) for n in (
        "mean_ready", "g_ready", "square_ready", "var_ready", "rstd_ready"))
    s_gt, s_gtc, s_y, s_yc, s_y1, s_y2, s_z, s_xz = (sem(n) for n in (
        "gT_in_psum", "gT_ready", "y_in_psum", "y_ready", "y_first_rest",
        "y_second_rest", "z_in_psum", "xz_ready"))
    s_counts, s_cnt, s_adj, s_prod, s_deg, s_inv, s_res, s_out = (sem(n) for n in (
        "counts_in_psum", "counts_ready", "adj_ready", "product_in_psum",
        "degrees_clamped", "inv_ready", "result_ready", "out_written"))
    s_dsum = [sem("degree_sums"), sem("degree_sums_3")]
    s_one = sem("one_ready")
    s_zc, s_rest = sem("z_ready"), [sem("degree_rests"), sem("degree_rest_3")]
    s_pair, s_degp = sem("degree_pairs"), sem("degrees_in_psum")
    s_bsum, s_counted, s_full, s_used, s_iall = (sem(n) for n in (
        "block_sums_in_psum", "counted_ready", "full_window_ready", "full_window_used", "iota_all_ready"))

    xv = x.rearrange("(k p) f -> p k f", p=P)
    ov = out.rearrange("(k p) f -> p k f", p=P)
    wv = wb.rearrange("(c p) f -> p c f", p=P)

    with nc.Block() as block:

        @block.sync
        def _(sp):
            sp.dma_start(ed[:, :, :], edges).then_inc(s_e, 16)
            sp.dma_start(xs[:, 2:KB, :], xv[:, 2:KB, :]).then_inc(s_x[1], 16)
            sp.dma_start(wbs[:, :, :], wv).then_inc(s_w, 16)

            def store(k, rnd):
                sp.wait_ge(s_res, rnd * KB + k + 1)
                sp.dma_start(ov[:, k, :], res[:, k, :]).then_inc(s_out, 16)

            for k in range(KB):
                store(k, 0)
            sp.wait_ge(s_out, 16 * KB)
            sp.wait_ge(s_counted, 1)
            with sp.If(sp.value_load(counted[0:1, 0:1], min_val=0, max_val=E) < E):
                for k in range(KB):
                    store(k, 1)
                sp.wait_ge(s_out, 32 * KB)

        @block.gpsimd
        def _(pool):
            pool.memset(zeros[:, :], 0.0).then_inc(s_zero, 1)
            pool.iota(middle[:, :], [[P, T]], base=P // 2, channel_multiplier=0).then_inc(s_middle, 1)
            pool.iota(iota[:, :], [[1, P]], base=0, channel_multiplier=0,
                      allow_small_or_imprecise_dtypes=True).then_inc(s_iota, 1)
            pool.memset(ones[:, :], 1.0).then_inc(s_ident, 1)
            pool.memset(one[:, :], 1.0).then_inc(s_one, 1)
            pool.memset(half[:, :], -0.5).then_inc(s_half, 1)
            pool.wait_ge(s_ident, 1)
            pool.affine_select(ident[:, :], ones[:, :], [[-1, P]], ALU.is_equal, 0.0, base=0,
                               channel_multiplier=1).then_inc(s_ident, 1)
            pool.wait_ge(s_half, 1)
            for pair in range(2):
                ks = slice(2 * pair, 2 * pair + 2)
                pool.wait_ge(s_sq, 2 * pair + 2)
                pool.tensor_scalar(var[:, ks], vsum[:, ks], 1.0 / D, EPS, ALU.mult,
                                   ALU.add).then_inc(s_var, 1)
                pool.wait_ge(s_var, pair + 1)
                pool.tensor_tensor(rstd[:, ks], var[:, ks], half[:, ks], ALU.pow).then_inc(s_rstd, 1)

            def split(i, pair):
                ks = slice(2 * pair, 2 * pair + 2)
                pool.tensor_tensor(parts[i + 1][:, ks, :], parts[i][:, ks, :], upper[i][:, ks, :],
                                   ALU.subtract).then_inc((s_y1, s_y2)[i], 1)

            def residual(pair):
                ks = slice(2 * pair, 2 * pair + 2)
                pool.wait_ge(s_x[pair], 16)
                pool.wait_ge(s_zc, 2 * pair + 2)
                pool.tensor_tensor(xz[:, ks, :], zs[:, ks, :], xs[:, ks, :], ALU.add).then_inc(s_xz, 1)

            def degree_sum(k, rnd):
                pool.wait_ge(s_cnt, rnd * KB + k + 1)
                if rnd:
                    pool.wait_ge(s_prod, KB)
                c = cnt[:, k, :].rearrange("p (d r) -> p d r", r=KB)
                pool.tensor_tensor(pairs[:, k, :, :], c[:, :, 0:2], c[:, :, 2:4], ALU.add).then_inc(s_pair, 1)
                pool.wait_ge(s_pair, rnd * (KB - 1) + k + 1)
                pool.tensor_tensor(dsum[:, k, :], pairs[:, k, :, 0], pairs[:, k, :, 1],
                                   ALU.add).then_inc(s_dsum[k == KB - 1], 1)
                pool.wait_ge(s_dsum[k == KB - 1], rnd + 1 if k == KB - 1 else rnd * (KB - 1) + k + 1)
                pool.tensor_tensor(drest[:, k, :], dsum[:, k, :], dtop[:, k, :],
                                   ALU.subtract).then_inc(s_rest[k == KB - 1], 1)

            for pair in range(2):
                pool.wait_ge(s_yc, 2 * pair + 2)
                split(0, pair)
                pool.wait_ge(s_y1, pair + 1)
                split(1, pair)
            degree_sum(0, 0)
            residual(0)
            degree_sum(1, 0)
            degree_sum(2, 0)
            residual(1)
            pool.wait_ge(s_counted, 1)
            with pool.If(pool.value_load(counted[0:1, 0:1], min_val=0, max_val=E) < E):
                pool.iota(iota_all[:, :], [[1, KB * COLS]], base=0, channel_multiplier=0,
                          allow_small_or_imprecise_dtypes=True).then_inc(s_iall, 1)
                for k in range(KB):
                    degree_sum(k, 1)

        @block.scalar
        def _(act):
            act.dma_start(xs[:, 0:2, :], xv[:, 0:2, :]).then_inc(s_x[0], 16)
            for k in range(KB):
                act.wait_ge(s_x[k // 2], 16)
                act.activation(scratch[:, k, :], xs[:, k, :], ACT.Copy, scale=-1.0 / D,
                               accum_out=nmean[:, k:k + 1]).then_inc(s_mean, 1)

            def squares(k):
                act.wait_ge(s_mean, k + 1)
                act.activation(scratch[:, KB + k, :], xs[:, k, :], ACT.Square, bias=nmean[:, k:k + 1],
                               accum_out=vsum[:, k:k + 1]).then_inc(s_sq, 1)

            def gt_out(pair):
                act.wait_ge(s_gt, pair + 1)
                act.activation(gT[:, pair, :, :].rearrange("p j n -> p (j n)"), py[pair][:, :],
                               ACT.Copy).then_inc(s_gtc, 1)

            def y_out(k):
                act.wait_ge(s_rstd, k // 2 + 1)
                act.wait_ge(s_y, k // 2 + 1)
                act.activation(parts[0][:, k, :], py[k // 2][:, k % 2 * D:k % 2 * D + D], ACT.Copy,
                               scale=rstd[:, k:k + 1]).then_inc(s_yc, 1)

            def z_out(k):
                act.wait_ge(s_rstd, k // 2 + 1)
                act.wait_ge(s_z, k // 2 + 1)
                act.activation(zs[:, k, :], pz[k // 2][:, k % 2 * D:k % 2 * D + D], ACT.Copy,
                               scale=rstd[:, k:k + 1]).then_inc(s_zc, 1)

            def counts_out(k, rnd):
                if rnd:
                    act.wait_ge(s_used, T + 1)
                    act.wait_ge(s_prod, KB)
                    act.activation(cnt[:, k, :], bank[k][:, :], ACT.Copy).then_inc(s_cnt, 1)
                else:
                    act.wait_ge(s_counts, k + 1)
                    act.activation(cnt[:, k, :], bank[k][:, :], ACT.Copy,
                                   accum_out=csum[:, k:k + 1]).then_inc(s_cnt, 1)
                act.activation(adj[:, k, :, :].rearrange("p d r -> p (d r)"), bank[k][:, :],
                               ACT.Sign).then_inc(s_adj, 1)

            squares(0)
            gt_out(0)
            squares(1)
            gt_out(1)
            squares(2)
            squares(3)
            y_out(0)
            y_out(1)
            y_out(2)
            y_out(3)
            counts_out(0, 0)
            z_out(0)
            z_out(1)
            z_out(2)
            z_out(3)
            for k in range(1, KB):
                counts_out(k, 0)
            act.wait_ge(s_bsum, 1)
            act.activation(totals[0:1, :], pz[0][0:1, 0:KB], ACT.Copy,
                           accum_out=total[0:1, :]).then_inc(s_total, 1)
            act.wait_ge(s_total, 1)
            act.activation(counted[0:1, 0:1], total[0:1, :], ACT.Copy).then_inc(s_counted, 1)
            act.wait_ge(s_counted, 1)
            with act.If(act.value_load(counted[0:1, 0:1], min_val=0, max_val=E) < E):
                for k in range(KB):
                    counts_out(k, 1)

        @block.vector
        def _(dve):
            dve.wait_ge(s_middle, 1)
            for a, z, w in RUNS:
                last = dve.tensor_scalar(base[:, a:z], middle[:, a:z], N / E, ROUND - w / 2,
                                         ALU.mult, ALU.add)
            last.then_inc(s_prep, 1)
            dve.wait_ge(s_prep, 1)
            dve.tensor_scalar(base[:, :], base[:, :], ROUND, 0.0, ALU.subtract,
                              ALU.max).then_inc(s_prep, 1)
            dve.wait_ge(s_prep, 2)
            dve.tensor_scalar(base[:, :], base[:, :], float(N - WIDTHS[-1]), float(KB), ALU.min,
                              ALU.mult).then_inc(s_prep, 1)

            dve.wait_ge(s_e, 16)
            low = ed[:, :, :].bitcast(i16).rearrange("p a (t h) -> p a t h", h=2)[:, 0, :, 0]
            dve.tensor_scalar(lo[:, :], low, P.bit_length() - 1, None,
                              ALU.logical_shift_right).then_inc(s_prep, 1)
            dve.tensor_scalar(hi2[:, :, :], low[:, :, None].to_broadcast([P, T, 2]), P - 1, None,
                              ALU.bitwise_and).then_inc(s_prep, 1)
            dve.wait_ge(s_prep, 4)
            dve.scalar_tensor_tensor(key[:, :], ed[:, 1, :], float(KB), lo[:, :],
                                     ALU.mult, ALU.add).then_inc(s_prep, 1)
            dve.wait_ge(s_iota, 1)

            def one_hot(c, out, idx, width):
                a, n, h = STARTS[c], CHUNKS[c], width // 2
                o = out.rearrange("p (t h two) -> p t h two", h=h, two=2)
                i0 = iota[:, 0:width].rearrange("p (h two) -> p h two", two=2)[:, None, :, :] \
                    .to_broadcast([P, n, h, 2])
                i1 = idx[:, a:a + n, None, :].to_broadcast([P, n, h, 2])
                return dve.tensor_tensor(o, i0, i1, ALU.is_equal)

            def centred(k):
                dve.wait_ge(s_mean, k + 1)
                dve.tensor_scalar(g[:, k, :], xs[:, k, :], nmean[:, k:k + 1], 0.0, ALU.add,
                                  ALU.max).then_inc(s_g, 1)

            def hi_one_hot(c):
                one_hot(c, hi_hot[:, STARTS[c]:STARTS[c + 1], :].rearrange("p t h -> p (t h)"),
                        hi2, P).then_inc(s_hi, 1)

            def lo_one_hot(c):
                one_hot(c, lo_hot[:, LO_AT[c]:LO_AT[c + 1]], rel2, WIDTHS[c] * KB).then_inc(s_lo, 1)

            def degree_sum(k):
                dve.wait_ge(s_cnt, k + 1)
                dve.tensor_reduce(dsum[:, k, :], cnt[:, k, :].rearrange("p (d r) -> p d r", r=KB),
                                  AX.X, ALU.add).then_inc(s_dsum[1], 1)

            def degree_rest(k):
                dve.wait_ge(s_dsum[1], 1)
                dve.tensor_tensor(drest[:, k, :], dsum[:, k, :], dtop[:, k, :],
                                  ALU.subtract).then_inc(s_rest[1], 1)

            def clamp(k, rnd):
                dve.wait_ge(s_degp, rnd * KB + k + 1)
                dve.tensor_scalar(degc[:, k:k + 1], py[k % 2][:, k:k + 1], 1.0, None,
                                  ALU.max).then_inc(s_deg, 1)

            def inverse(k, rnd):
                dve.wait_ge(s_deg, rnd * KB + k + 1)
                dve.reciprocal(inv[:, k:k + 1], degc[:, k:k + 1]).then_inc(s_inv, 1)

            def result(k, rnd):
                n = rnd * KB + k
                dve.wait_ge(s_prod, n + 1)
                dve.wait_ge(s_inv, n + 1)
                dve.wait_ge(s_xz, k // 2 + 1)
                if rnd:
                    dve.wait_ge(s_out, 16 * KB)
                dve.scalar_tensor_tensor(res[:, k, :], bank[k][:, 0:D], inv[:, k:k + 1],
                                         xz[:, k, :], ALU.mult, ALU.add).then_inc(s_res, 1)

            dve.wait_ge(s_prep, 5)
            hi_one_hot(0)
            dve.wait_ge(s_prep, 6)
            dve.tensor_tensor(rel2[:, :, :], key[:, :, None].to_broadcast([P, T, 2]),
                              base[:, :, None].to_broadcast([P, T, 2]), ALU.subtract).then_inc(s_rel, 1)
            centred(0)
            dve.wait_ge(s_rel, 1)
            lo_one_hot(0)
            centred(1)
            hi_one_hot(1)
            centred(2)
            centred(3)
            lo_one_hot(1)
            for c in range(2, len(CHUNKS)):
                hi_one_hot(c)
                lo_one_hot(c)
            clamp(0, 0)
            clamp(1, 0)
            inverse(0, 0)
            inverse(1, 0)
            result(0, 0)
            result(1, 0)
            degree_sum(KB - 1)
            clamp(2, 0)
            inverse(2, 0)
            degree_rest(KB - 1)
            result(2, 0)
            clamp(3, 0)
            inverse(3, 0)
            result(3, 0)

            dve.wait_ge(s_counted, 1)
            with dve.If(dve.value_load(counted[0:1, 0:1], min_val=0, max_val=E) < E):
                dve.wait_ge(s_iall, 1)
                with dve.Fori(0, T) as t:
                    dve.wait_ge(s_used, t + 1)
                    dve.tensor_scalar(lo_full[:, :], iota_all[:, :], key[:, bass.ds(t, 1)], None,
                                      ALU.is_equal).then_inc(s_full, 1)
                for k in range(KB):
                    clamp(k, 1)
                    inverse(k, 1)
                    result(k, 1)

        @block.tensor
        def _(pe):
            def clear_counts():
                for k in range(KB):
                    pe.matmul(bank[k][:, :], zeros[:, 0:P], zeros[:, :], start=True, stop=False,
                              skip_group_check=True)

            def tile(t):
                c, (b, w) = chunk_of(t), window(t)
                at = LO_AT[c] + (t - STARTS[c]) * w * KB
                cut = min(w, (b // P + 1) * P - b)
                for d0, d1 in ((0, cut), (cut, w)):
                    if d0 < d1:
                        k, c0 = (b + d0) // P, (b + d0) % P * KB
                        last = pe.matmul(bank[k][:, c0:c0 + (d1 - d0) * KB], hi_hot[:, t, :],
                                         lo_hot[:, at + d0 * KB:at + d1 * KB], start=False,
                                         stop=False, skip_group_check=True)
                if t in LAST_TILE:
                    last.then_inc(s_counts, 1)

            def transposes(k):
                pe.wait_ge(s_g, k + 1)
                for j in range(FC):
                    at = (2 * j + k % 2) * P
                    m = pe.transpose(py[k // 2][:, at:at + P], g[:, k, j * P:(j + 1) * P], ident[:, :])
                if k % 2:
                    m.then_inc(s_gt, 1)

            def dense(pair, ps, half, done):
                pe.wait_ge(s_gtc, pair + 1)
                for k in range(2):
                    for j in range(FC):
                        m = pe.matmul(ps[pair][:, k * D:k * D + D], gT[:, pair, j, k * P:(k + 1) * P],
                                      wbs[:, j, half * D:half * D + D], start=(j == 0),
                                      stop=(j == FC - 1))
                m.then_inc(done, 1)

            def edges_counted():
                pe.wait_ge(s_cnt, KB)
                pe.wait_ge(s_zc, 2)
                pe.matmul(pz[0][0:1, 0:KB], ones[:, 0:1], csum[:, :], start=True, stop=True).then_inc(s_bsum, 1)

            def degrees(k, rnd):
                n = rnd * KB + k
                pe.wait_ge(s_one, 1)
                if k < KB - 1:
                    pe.wait_ge(s_rest[0], rnd * (KB - 1) + k + 1)
                else:
                    pe.wait_ge(s_rest[1], rnd + 1)
                if n >= 2:
                    pe.wait_ge(s_deg, n - 1)
                pe.matmul(py[k % 2][:, k:k + 1], dtop[:, k, :], one[:, 0:1], start=True, stop=False)
                pe.matmul(py[k % 2][:, k:k + 1], drest[:, k, :], one[:, 0:1], start=False,
                          stop=True).then_inc(s_degp, 1)

            def product(k, rnd, parts=range(3)):
                n = rnd * KB + k
                pe.wait_ge(s_adj, n + 1)
                for i in parts:
                    for r in range(KB):
                        if r % 2 == 0:
                            pe.wait_ge((s_yc, s_y1, s_y2)[i], (r + 2, r // 2 + 1)[i > 0])
                        m = pe.matmul(bank[k][:, 0:D], adj[:, k, :, r], upper[i][:, r, :],
                                      start=(i == 0 and r == 0), stop=(i == 2 and r == KB - 1))
                if i == 2:
                    m.then_inc(s_prod, 1)

            def tiles(*chunks):
                for c in chunks:
                    pe.wait_ge(s_hi, c + 1)
                    pe.wait_ge(s_lo, c + 1)
                    for t in range(STARTS[c], STARTS[c + 1]):
                        tile(t)

            pe.wait_ge(s_zero, 1)
            for _ in range(CLEARS):
                clear_counts()
            pe.wait_ge(s_ident, 2)
            transposes(0)
            transposes(1)
            transposes(2)
            transposes(3)
            pe.wait_ge(s_w, 16)
            dense(0, py, 0, s_y)
            dense(1, py, 0, s_y)
            tiles(0, 1, 2, 3, 4)
            dense(0, pz, 1, s_z)
            dense(1, pz, 1, s_z)
            tiles(5, 6, 7, 8)
            product(0, 0)
            tiles(9)
            degrees(0, 0)
            product(1, 0)
            tiles(10)
            degrees(1, 0)
            tiles(11, 12)
            product(2, 0)
            degrees(2, 0)
            product(3, 0, range(2))
            degrees(3, 0)
            product(3, 0, range(2, 3))
            edges_counted()

            pe.wait_ge(s_counted, 1)
            with pe.If(pe.value_load(counted[0:1, 0:1], min_val=0, max_val=E) < E):
                pe.wait_ge(s_res, KB)
                clear_counts()
                pe.nop().then_inc(s_used, 1)
                with pe.Fori(0, T) as t:
                    pe.wait_ge(s_full, t + 1)
                    for k in range(KB):
                        m = pe.matmul(bank[k][:, :], hi_hot[:, bass.ds(t, 1), :].rearrange("p a b -> p (a b)"),
                                      lo_full[:, k * COLS:(k + 1) * COLS], start=False,
                                      stop=False, skip_group_check=True)
                    m.then_inc(s_used, 1)
                for k in range(KB):
                    product(k, 1)
                    degrees(k, 1)


def kernel(**inputs):
    import numpy as np
    import concourse.bacc as bacc
    from concourse.bass_utils import run_bass_kernel_spmd

    x = np.ascontiguousarray(inputs["x"])
    w, b = np.asarray(inputs["L0_gnn_W"]), np.asarray(inputs["L0_gnn_B"])
    arrays = {
        "edges": np.ascontiguousarray(np.stack(
            [np.asarray(inputs[n]).reshape(T, P).T for n in ("src", "dst")], axis=1)),
        "x": x,
        "wb": np.ascontiguousarray(np.concatenate([w.T, b.T], axis=1)),
    }
    nc = bacc.Bacc("TRN2", target_bir_lowering=False, num_devices=1)
    aps = [nc.dram_tensor(n, a.shape, mybir.dt.from_np(a.dtype), kind="ExternalInput").ap()
           for n, a in arrays.items()]
    out = nc.dram_tensor("out", (N, D), mybir.dt.float32, kind="ExternalOutput").ap()
    build(nc, *aps, out)
    return run_bass_kernel_spmd(nc, [arrays], core_ids=[0]).results[0]["out"]
```
